# Optimizing a Trainium2 kernel written in Bass

```python
import numpy as np
import jax
import jax.numpy as jnp

def _softmax(x, axis=-1):
    return jax.nn.softmax(x, axis=axis)

def _gelu(x):
    return jax.nn.gelu(x, approximate=True)

def _silu(x):
    return jax.nn.silu(x)

def _sigmoid(x):
    return jax.nn.sigmoid(x)

def _layernorm(x, axis=-1, eps=1e-05):
    m = jnp.mean(x, axis=axis, keepdims=True)
    v = jnp.var(x, axis=axis, keepdims=True)
    return (x - m) / jnp.sqrt(v + eps)

def _scatter_add(tgt, idx, src, axis=0):
    return tgt.at[idx].add(src)

def _segment_sum(src, seg, n):
    return jax.ops.segment_sum(src, seg, n)
kernel_name = 'mk_adaln_d1_jaxref_r8_f9248b'

def setup_inputs(seed: int=0):
    np.random.seed(seed)
    _w = jnp.asarray

    def _L0_attn_setup():
        import jax, jax.numpy as jnp
        import numpy as np
        D_MODEL, D_QKV, N_HEADS = (128, 64, 16)
        key = jax.random.key(seed)
        k_x, k_qkv, k_out = jax.random.split(key, 3)
        X = jax.random.normal(k_x, (2, 256, D_MODEL), dtype=jnp.float32)
        W_qkv = jax.random.normal(k_qkv, (D_MODEL, 3 * D_QKV * N_HEADS), dtype=jnp.float32) * D_MODEL ** (-0.5)
        W_out = jax.random.normal(k_out, (D_QKV * N_HEADS, D_MODEL), dtype=jnp.float32) * (D_QKV * N_HEADS) ** (-0.5)
        return {'X': X, 'W_qkv': W_qkv, 'W_out': W_out}
    _L0_attn_in = _L0_attn_setup()

    def _L0_ffn_setup():
        import jax, jax.numpy as jnp
        import numpy as np
        E = 8
        TOP_K = 2
        DIM = 128
        HID = 256
        key = jax.random.key(seed)
        k1, k2, k3, k4, k5 = jax.random.split(key, 5)
        s = 0.02
        x = jax.random.normal(k1, (2, 256, DIM), dtype=jnp.float32)
        Wg = jax.random.normal(k2, (DIM, E), dtype=jnp.float32) * s
        W1 = jax.random.normal(k3, (E, DIM, HID), dtype=jnp.float32) * s
        W2 = jax.random.normal(k4, (E, DIM, HID), dtype=jnp.float32) * s
        W3 = jax.random.normal(k5, (E, HID, DIM), dtype=jnp.float32) * s
        return {'x': x, 'Wg': Wg, 'W1': W1, 'W2': W2, 'W3': W3}
    _L0_ffn_in = _L0_ffn_setup()
    _L0_c = _w((lambda *s: np.random.randn(*s).astype(np.float32) * 0.05)(1, 128))
    _L0_wmod = _w((lambda *s: np.random.randn(*s).astype(np.float32) * 0.05)(128, 6 * 128) * 128 ** (-0.5))
    _d = {'L0_attn_X': _L0_attn_in['X'], 'L0_attn_W_qkv': _L0_attn_in['W_qkv'], 'L0_attn_W_out': _L0_attn_in['W_out'], 'L0_ffn_Wg': _L0_ffn_in['Wg'], 'L0_ffn_W1': _L0_ffn_in['W1'], 'L0_ffn_W2': _L0_ffn_in['W2'], 'L0_ffn_W3': _L0_ffn_in['W3'], 'L0_c': _L0_c, 'L0_wmod': _L0_wmod}
    _x0 = _d['L0_attn_X']
    _d['L0_attn_X'] = jax.random.normal(jax.random.fold_in(jax.random.key(seed), 1), (1, 2048, 128), dtype=_x0.dtype)
    del _x0
    return _d

def reference(L0_attn_X, L0_attn_W_qkv, L0_attn_W_out, L0_ffn_Wg, L0_ffn_W1, L0_ffn_W2, L0_ffn_W3, L0_c, L0_wmod):

    def _L0_attn_ref(X, W_qkv, W_out):
        import jax, jax.numpy as jnp
        import numpy as np
        D_MODEL, D_QKV, N_HEADS = (128, 64, 16)
        b, s, _ = X.shape
        h, d = (N_HEADS, D_QKV)
        scale = d ** 0.5
        qkv = X @ W_qkv
        qkv = qkv.reshape(b, s, h, d, 3)
        q, k, v = (qkv[..., 0], qkv[..., 1], qkv[..., 2])
        scores = jnp.einsum('bqhd,bkhd->bhqk', q, k) / scale
        weights = jax.nn.softmax(scores, axis=-1)
        attn = jnp.einsum('bhqk,bkhd->bqhd', weights, v)
        return attn.reshape(b, s, h * d) @ W_out

    def _L0_ffn_ref(x, Wg, W1, W2, W3):
        import jax, jax.numpy as jnp
        import numpy as np
        E = 8
        TOP_K = 2
        DIM = 128
        HID = 256
        B, T, C = x.shape
        xf = x.reshape(-1, C)
        logits = xf @ Wg
        top_w, top_i = jax.lax.top_k(logits, TOP_K)
        top_w = jax.nn.softmax(top_w, axis=-1)
        one_hot = jax.nn.one_hot(top_i, E, dtype=xf.dtype)
        combine = jnp.einsum('nk,nke->ne', top_w, one_hot)
        h = jnp.einsum('nc,ech->enh', xf, W1)
        g = jnp.einsum('nc,ech->enh', xf, W2)
        y = jnp.einsum('enh,ehc->enc', jax.nn.silu(h) * g, W3)
        out = jnp.einsum('enc,ne->nc', y, combine)
        return out.reshape(B, T, C)
    x = L0_attn_X
    mod = (_silu(L0_c) @ L0_wmod).reshape(L0_c.shape[0], 6, 1, -1)
    sa, ca, ga, sb, cb, gb = (mod[:, 0], mod[:, 1], mod[:, 2], mod[:, 3], mod[:, 4], mod[:, 5])
    ga = (2 * (ga >= 0) - 1) * jnp.maximum(jnp.abs(ga), 0.25)
    gb = (2 * (gb >= 0) - 1) * jnp.maximum(jnp.abs(gb), 0.25)
    h = _layernorm(x, axis=-1) * (1 + ca) + sa
    x = x + ga * _L0_attn_ref(h, L0_attn_W_qkv, L0_attn_W_out)
    h = _layernorm(x, axis=-1) * (1 + cb) + sb
    x = x + gb * _L0_ffn_ref(h, L0_ffn_Wg, L0_ffn_W1, L0_ffn_W2, L0_ffn_W3)
    return x

_drawn_inputs = setup_inputs


def setup_inputs(seed=0):
    import zlib

    import numpy as np

    out = dict(_drawn_inputs(seed))
    spreads = {}
    factors = {'L0_ffn_Wg': 8.0, 'L0_ffn_W1': 8.0, 'L0_ffn_W2': 8.0, 'L0_ffn_W3': 8.0}
    for name, (base, spread) in spreads.items():
        noise = np.random.default_rng([zlib.crc32(name.encode()), seed]).standard_normal(out[name].shape)
        drawn = base * np.exp(spread * noise) if base else spread * noise
        out[name] = jnp.asarray(drawn.astype(out[name].dtype))
    for name, factor in factors.items():
        out[name] = (out[name] * factor).astype(out[name].dtype)
    return out
```

```python
from contextlib import ExitStack

import concourse.bass as bass
from concourse import mybir

F32 = mybir.dt.float32
F32R = mybir.dt.float32r
ALU = mybir.AluOpType
ACT = mybir.ActivationFunctionType
AX_X = mybir.AxisListType.X

P = 128
BANK = 512
HEADS = 16
DH = 64
EPS = 1e-5
NEVER = -3.0e38
TOP = 0.25

DVE_KTS = (11, 15)
POOL_ADDS = {kt: max(n, 1) for n, kt in enumerate(kt for kt in range(16) if kt not in DVE_KTS)}
POOL_PER_HALF = max(POOL_ADDS.values())
PT_RING = 4
RING = 3
NCHUNK = 4
KT = 16
STEPS = 2 * KT
DEN_AT = 3
OUT_AT = 11
PROJ_AT = (0, 2, 5, 7)
TURN_AT = 30
MAX_FILLS = 4 * KT
MAX_BLOCKS = (0,) * 9 + (3, 4, 2, 3, 4, 4, 4) + (2, 2, 4, 3, 3, 3, 3, 3, 3, 3, 3, 3, 3, 2, 0, 0)
assert sum(MAX_BLOCKS) == MAX_FILLS and len(MAX_BLOCKS) == STEPS


def aux_work(t, prepare, prior, prior_odd):
    kt = t % KT
    work = []
    if prepare and t in PROJ_AT:
        work.append(("project", PROJ_AT.index(t)))
    if kt == DEN_AT and prior:
        work.append(("sums", 0))
    if kt == OUT_AT and prior and prior_odd:
        work += [("output", 0), ("output", 1)]
    if prepare:
        done = sum(MAX_BLOCKS[:t])
        work += [("maximum", m) for m in range(done, done + MAX_BLOCKS[t])]
    if prepare and t == TURN_AT:
        work.append(("turn", 0))
    return work


def layer(nc, X, W_qkv, W_out, Wg, W1, W2, W3, C, Wmod, out):
    tokens, D = X.shape[1], X.shape[2]
    E, _, HID = W1.shape
    TT = tokens // P
    HH = HID // P
    PAIRS = HEADS // 2
    assert D == P and tokens == NCHUNK * BANK and HEADS * DH == W_out.shape[0] and HH == 2 and TT == KT

    FILLS_MOD, FILLS_LN = 1, TT // 4
    FILLS_PREP = NCHUNK + MAX_FILLS + 1

    def head_work(i, par, t):
        begins = isinstance(i, int) and i == 0
        ends = isinstance(i, int) and i == PAIRS - 1
        half = 2 * par + t // KT
        return aux_work(t, not (ends and par == 1), not (begins and half == 0), half in (0, 3))

    FILLS_FIRST = sum(len(head_work(0, par, t)) for par in range(2) for t in range(STEPS))
    FILLS_TURN = sum(len(head_work(1, par, t)) for par in range(2) for t in range(STEPS))
    PROLOGUE = FILLS_MOD + FILLS_LN + FILLS_PREP

    def turn_fills(i):
        if isinstance(i, int) and i == 0:
            return PROLOGUE
        return PROLOGUE + FILLS_FIRST - FILLS_TURN + FILLS_TURN * i

    LAST = PAIRS * FILLS_TURN + PROLOGUE + FILLS_FIRST - FILLS_TURN - FILLS_PREP

    ctx = ExitStack()
    with ctx:
        def sb(name, shape, dt=F32):
            return ctx.enter_context(nc.sbuf_tensor(name, shape, dt))

        def sem(name):
            return ctx.enter_context(nc.semaphore(name))

        x = sb("x", [P, TT, D])
        hT = sb("hT", [P, tokens])
        v_all = sb("v_all", [P, HEADS, KT * DH])
        khl = [sb(f"khl{n}", [P, tokens], F32R) for n in range(2)]
        kh1 = [sb(f"kh1{n}", [DH + 1, tokens], F32R) for n in range(2)]
        qhh = [sb(f"qhh{n}", [P, tokens], F32R) for n in range(2)]
        qlm = [sb(f"qlm{n}", [DH + 1, tokens], F32R) for n in range(2)]
        v_h = [sb(f"v_h{n}", [P, KT, DH]) for n in range(2)]
        probs = sb("probs", [P, PT_RING, 2 * BANK])
        w_qkv = probs[:, 0:3, :].rearrange("p a b -> p (a b)")
        sum_pool = sb("sum_pool", [P, 2 * BANK])
        sum_dve = sb("sum_dve", [P, 2 * BANK])
        attn = sb("attn", [P, NCHUNK, BANK])
        y = sb("y", [P, tokens])
        rden = sb("rden", [P, BANK])
        w_head = [sb(f"w_head{n}", [P, 2 * DH]) for n in range(2)]
        wo_pair = sb("wo_pair", [P, 2, D])
        wmod = sb("wmod", [P, 6 * D])
        den = wmod[:, 0:BANK]
        ident = sb("ident", [P, P])
        ones = sb("ones", [P, P])
        silu_c = sb("silu_c", [P, 4])
        c_wide = sb("c_wide", [P, P])
        mods = sb("mods", [P, 8])
        modt = sb("modt", [P, 8])
        gb_row = sb("gb_row", [P, D])
        gb_tmp = sb("gb_tmp", [P, 2 * D])
        rank = sb("rank", [P, TT, E])
        stats = sb("stats", [P, TT, 6])
        mv = sb("mv", [P, TT, 2])
        rstd, var, std = sb("rstd", [P, TT]), sb("var", [P, TT]), sb("std", [P, TT])
        xn = sb("xn", [P, 4, D])
        max4 = sb("max4", [P, KT, NCHUNK])
        maxq = sb("maxq", [P, KT])
        neg_max = sb("neg_max", [KT, P], F32R)

        score = ctx.enter_context(nc.psum_tensor("score", [P, RING, BANK], F32))
        out_acc = ctx.enter_context(nc.psum_tensor("out_acc", [P, 2, BANK], F32))
        aux = ctx.enter_context(nc.psum_tensor("aux", [P, RING, BANK], F32))

        flat = v_all[:, :, :].rearrange("p h n -> p (h n)")
        w1_sb = flat[:, 0:2048].rearrange("p (e n) -> p e n", e=E)
        w2_sb = flat[:, 2048:4096].rearrange("p (e n) -> p e n", e=E)
        w3_sb = flat[:, 4096:6144].rearrange("p (e n) -> p e n", e=E * HH)
        w3_raw = flat[:, 6144:8192].rearrange("p (e n) -> p e n", e=E * HH)
        up = flat[:, 8192:10240].rearrange("p (b h n) -> p b h n", b=2, h=HH)
        silu_g = flat[:, 10240:11264].rearrange("p (b n) -> p b n", b=2)
        moe = flat[:, 11264:11776].rearrange("p (t n) -> p t n", t=4)
        wg_sb = flat[:, 11776:11784]
        lg = flat[:, 11800:11928].rearrange("p (t e) -> p t e", e=E)
        lg2 = flat[:, 11928:12056].rearrange("p (t e) -> p t e", e=E)
        key = flat[:, 12056:12184].rearrange("p (t e) -> p t e", e=E)
        hot1 = flat[:, 12184:12312].rearrange("p (t e) -> p t e", e=E)
        hot2 = flat[:, 12312:12440].rearrange("p (t e) -> p t e", e=E)
        comb = flat[:, 12440:12568].rearrange("p (t e) -> p t e", e=E)
        comb_j = flat[:, 12696:12728].rearrange("p (t e) -> p t e", e=E)
        top1, top2, pick, dlt, wt1, wt2 = (flat[:, 12728 + TT * n:12728 + TT * (n + 1)] for n in range(6))

        modulation_in, x_in, w_qkv_in = sem("modulation_in"), sem("x_in"), sem("w_qkv_in")
        w_head_in = [sem("w_head_in0"), sem("w_head_in1")]
        v_in, wo_in, row_in, ffn_in = sem("v_in"), sem("wo_in"), sem("row_in"), sem("ffn_in")
        consts = sem("consts")
        exp_c = sem("exp_c")
        silu_c_ok = sem("silu_c_ok")
        var_ok = sem("var_ok")
        std_ok = sem("std_ok")
        tile_ok = sem("tile_ok")
        fill = sem("fill")
        freed = sem("freed")
        v_fill = sem("v_fill")
        v_ok = sem("v_ok")
        high_ok = sem("high_ok")
        max_ok = sem("max_ok")
        scored = sem("scored")
        expd = sem("expd")
        pv_ok = sem("pv_ok")
        pool_sum = sem("pool_sum")
        dve_sum = sem("dve_sum")
        sums_ok = sem("sums_ok")
        inverted = sem("inverted")
        normed = sem("normed")
        logits_ok = sem("logits_ok")
        exp_ok = sem("exp_ok")
        weights_ok = sem("weights_ok")
        chunk_ok = sem("chunk_ok")
        hg_ok = sem("hg_ok")
        silu_ok = sem("silu_ok")
        up_ok = sem("up_ok")
        down_ok = sem("down_ok")
        moe_ok = sem("moe_ok")
        stored = sem("stored")
        dve_did = sem("dve_did")

        block = ctx.enter_context(nc.Block())
        wo_rows = W_out.rearrange("(a d) c -> a d c", d=DH)

        def pair_loop(eng, body):
            body(0)
            with eng.Fori(1, PAIRS - 1) as i:
                body(i)
            body(PAIRS - 1)

        def chunk_loop(eng, body):
            body(0)
            with eng.Fori(1, NCHUNK) as j:
                body(j)

        def is_first(i):
            return isinstance(i, int) and i == 0

        def is_last(i):
            return isinstance(i, int) and i == PAIRS - 1

        @block.sync
        def _(sp):
            sp.dma_start(silu_c[:, 0:1], C.rearrange("a d -> d a")).then_inc(modulation_in, 16)
            sp.dma_start(wmod[:, :], Wmod).then_inc(modulation_in, 16)
            sp.dma_start(x[:, :, :], X[0].rearrange("(t p) c -> p t c", p=P)).then_inc(x_in, 16)
            sp.dma_start(w_qkv, W_qkv).then_inc(w_qkv_in, 16)
            for n in range(2):
                sp.dma_start(w_head[n][:, :], W_qkv[:, 3 * DH * n:3 * DH * n + 2 * DH]).then_inc(w_head_in[n], 16)

            def max_row(n):
                sp.dma_start(qlm[n][DH:DH + 1, :].bitcast(F32), neg_max[:, :].bitcast(F32)
                             ).then_inc(row_in, 16)

            sp.wait_ge(v_ok, 2 * TT)
            sp.dma_start(v_h[0][:, :, :].rearrange("p k d -> p (k d)"), v_all[:, 0, :]).then_inc(v_in, 16)
            sp.wait_ge(freed, PROLOGUE)
            max_row(0)

            def body(i):
                k, moved = 0, turn_fills(i)
                for par in range(2):
                    nxt = 1 - par
                    if not is_last(i):
                        sp.wait_ge(freed, k + moved)
                        sp.dma_start(w_head[par][:, :], W_qkv[:, bass.ds(6 * DH * i + 3 * DH * (par + 2), 2 * DH)]
                                     ).then_inc(w_head_in[par], 16)
                    if not (is_last(i) and par == 1):
                        if not (is_first(i) and par == 0):
                            sp.wait_ge(pv_ok, 64 * i + 32 * par)
                        sp.dma_start(v_h[nxt][:, :, :].rearrange("p k d -> p (k d)"),
                                     v_all[:, bass.ds(2 * i + par + 1, 1), :].rearrange("p a n -> p (a n)")
                                     ).then_inc(v_in, 16)
                    for t in range(STEPS):
                        k += len(head_work(i, par, t))
                        if par == 0 and t == OUT_AT:
                            sp.wait_ge(freed, k + moved)
                            for s in range(2):
                                for n in range(2):
                                    sp.dma_start(wo_pair[DH * n:DH * (n + 1), s, :],
                                                 wo_rows[bass.ds(2 * i + (n ^ s), 1), :, :]
                                                 .rearrange("a d c -> (a d) c")).then_inc(wo_in, 16)
                    if not (is_last(i) and par == 1):
                        sp.wait_ge(freed, k + moved)
                        max_row(nxt)

            pair_loop(sp, body)
            sp.wait_ge(v_in, 16 * HEADS)
            sp.dma_start(wg_sb, Wg).then_inc(ffn_in, 16)
            sp.dma_start(w1_sb, W1.rearrange("e c n -> c e n")).then_inc(ffn_in, 16)
            sp.dma_start(w2_sb, W2.rearrange("e c n -> c e n")).then_inc(ffn_in, 16)
            sp.dma_start(w3_raw, W3.rearrange("e (h p) c -> p (e h) c", p=P)).then_inc(ffn_in, 16)
            out_chunks = out[0].rearrange("(j t p) c -> j p t c", p=P, t=4)

            def store(j):
                sp.wait_ge(moe_ok, E * j + E)
                sp.dma_start(out_chunks[bass.ds(j, 1), :, :, :].rearrange("j p t c -> (j p) t c"), moe
                             ).then_inc(stored, 16)

            chunk_loop(sp, store)
            sp.wait_ge(stored, 16 * NCHUNK)

        @block.gpsimd
        def _(pool):
            pool.memset(ones[:, :], 1.0).then_inc(consts, 1)
            pool.memset(ident[:, :], 0.0).then_inc(consts, 1)
            for e in range(E):
                pool.memset(rank[:, :, e], float(E - e)).then_inc(consts, 1)
            pool.wait_ge(consts, 2)
            pool.affine_select(out=ident[:, :], in_=ident[:, :], compare_op=ALU.not_equal, fill=1.0, base=0,
                               pattern=[[-1, P]], channel_multiplier=1).then_inc(consts, 1)

            def body(i):
                for half in range(4):
                    done = POOL_PER_HALF * (4 * i + half)
                    for kt in sorted(POOL_ADDS)[1:]:
                        pool.wait_ge(expd, 128 * i + 32 * half + 2 * kt + 2)
                        if not (is_first(i) and half == 0 and kt == 1):
                            pool.wait_ge(pool_sum, done + POOL_ADDS[kt] - 1)
                        if kt > 1:
                            pool.tensor_tensor(sum_pool[:, :], sum_pool[:, :], probs[:, kt % PT_RING, :], ALU.add
                                               ).then_inc(pool_sum, 1)
                            continue
                        if not (is_first(i) and half == 0):
                            pool.wait_ge(sums_ok, 4 * i + half)
                        pool.tensor_tensor(sum_pool[:, :], probs[:, 0, :], probs[:, 1, :], ALU.add
                                           ).then_inc(pool_sum, 1)

            pair_loop(pool, body)

        @block.scalar
        def _(act):
            act.wait_ge(modulation_in, 32)
            act.activation(silu_c[:, 1:2], silu_c[:, 0:1], ACT.Exp, scale=-1.0).then_inc(exp_c, 1)
            act.wait_ge(var_ok, 1)
            act.sqrt(std[:, :], var[:, :]).then_inc(std_ok, 1)

            def high_parts(n, c, k, moved):
                cols = slice(c * BANK, (c + 1) * BANK)
                act.wait_ge(fill, k + moved + 1)
                act.copy(qhh[n][0:DH, cols], aux[0:DH, k % RING, :])
                act.copy(qhh[n][DH:P, cols], aux[0:DH, k % RING, :])
                act.copy(kh1[n][0:DH, cols], aux[DH:P, k % RING, :])
                act.copy(khl[n][0:DH, cols], aux[DH:P, k % RING, :]).then_inc(high_ok, 1)

            for c in range(NCHUNK):
                high_parts(0, c, FILLS_MOD + FILLS_LN + c, 0)
            for n in range(2 * TT):
                t, g = divmod(n, 2)
                act.wait_ge(v_fill, n + 1)
                act.copy(v_all[:, 8 * g:8 * g + 8, DH * t:DH * (t + 1)],
                         score[:, n % RING, :].rearrange("p (h d) -> p h d", d=DH)).then_inc(v_ok, 1)

            def slot_free(i, half, kt):
                if is_first(i) and half == 0 and kt < PT_RING:
                    return
                act.wait_ge(pv_ok, 64 * i + 16 * half + kt - PT_RING + 1)
                old, before = (kt - PT_RING, 4 * i + half) if kt >= PT_RING else (kt - PT_RING + KT, 4 * i + half - 1)
                if old in POOL_ADDS:
                    act.wait_ge(pool_sum, POOL_PER_HALF * before + POOL_ADDS[old])
                else:
                    act.wait_ge(dve_sum, len(DVE_KTS) * before + DVE_KTS.index(old) + 1)

            def body(i):
                k, moved = 0, turn_fills(i)
                for par in range(2):
                    for t in range(STEPS):
                        for c in range(2):
                            act.wait_ge(scored, 128 * i + 64 * par + 2 * t + c + 1)
                            if c == 0:
                                slot_free(i, 2 * par + t // KT, t % KT)
                            act.activation(probs[:, t % PT_RING, BANK * c:BANK * (c + 1)],
                                           score[:, (par + 2 * t + c) % RING, :], ACT.Exp, scale=DH ** -0.5
                                           ).then_inc(expd, 1)
                        for what, n in head_work(i, par, t):
                            if what == "project":
                                high_parts(1 - par, n, k, moved)
                            k += 1

            pair_loop(act, body)
            act.wait_ge(var_ok, 2)
            act.sqrt(std[:, :], var[:, :]).then_inc(std_ok, 1)
            act.wait_ge(logits_ok, 1)
            act.activation(wt2[:, :], dlt[:, :], ACT.Exp).then_inc(exp_ok, 1)

            def gates(j):
                for b in range(E * HH):
                    act.wait_ge(hg_ok, E * HH * j + b + 1)
                    if not (is_first(j) and b < 2):
                        act.wait_ge(up_ok, E * HH * j + b - 1)
                    act.activation(silu_g[:, b % 2, :], score[:, b % 2, :], ACT.Silu).then_inc(silu_ok, 1)

            chunk_loop(act, gates)

        @block.vector
        def _(dve):
            did = [0]

            def link(ins):
                did[0] += 1
                ins.then_inc(dve_did, 1)
                dve.wait_ge(dve_did, did[0])

            def normalise(t):
                dve.tensor_scalar(xn[:, t % 4, :], x[:, t, :], mv[:, t, 0:1], rstd[:, t:t + 1],
                                  ALU.subtract, ALU.mult).then_inc(tile_ok, 1)

            def statistics(n):
                for t in range(TT - 1):
                    dve.bn_stats(stats[:, t, :], x[:, t, :])
                link(dve.bn_stats(stats[:, TT - 1, :], x[:, TT - 1, :]))
                for t in range(TT - 1):
                    dve.bn_aggr(mv[:, t, :], stats[:, t, :])
                link(dve.bn_aggr(mv[:, TT - 1, :], stats[:, TT - 1, :]))
                dve.tensor_scalar_add(var[:, :], mv[:, :, 1], EPS).then_inc(var_ok, 1)
                dve.wait_ge(std_ok, n)
                link(dve.reciprocal(rstd[:, :], std[:, :]))
                link(dve.tensor_tensor(std[:, :], rstd[:, :], rstd[:, :], ALU.mult))
                link(dve.tensor_tensor(std[:, :], std[:, :], var[:, :], ALU.mult))
                link(dve.tensor_scalar(std[:, :], std[:, :], -0.5, 1.5, ALU.mult, ALU.add))
                link(dve.tensor_tensor(rstd[:, :], rstd[:, :], std[:, :], ALU.mult))
                for t in range(4):
                    normalise(t)

            def modulated(k, shift, scale):
                for q in range(TT // 4):
                    dve.wait_ge(fill, k + q + 1)
                    dve.tensor_scalar(hT[:, q * BANK:(q + 1) * BANK], aux[:, (k + q) % RING, :],
                                      mods[:, scale:scale + 1], mods[:, shift:shift + 1],
                                      ALU.mult, ALU.add).then_inc(freed, 1)
                    for t in range(4 * (q + 1), min(4 * (q + 2), TT)):
                        normalise(t)

            def floor_gate(gate, tmp, size):
                link(dve.scalar_tensor_tensor(out=size, in0=gate, scalar=-1.0, in1=gate, op0=ALU.mult, op1=ALU.max))
                link(dve.tensor_scalar(tmp, gate, 0.0, 2.0, ALU.is_ge, ALU.mult))
                link(dve.tensor_scalar(size, size, TOP, None, ALU.max))
                link(dve.scalar_tensor_tensor(out=gate, in0=tmp, scalar=-1.0, in1=size, op0=ALU.add, op1=ALU.mult))

            for n in range(2):
                dve.memset(kh1[n][DH:DH + 1, :].bitcast(F32), 1.0)
            dve.wait_ge(exp_c, 1)
            link(dve.tensor_scalar_add(silu_c[:, 2:3], silu_c[:, 1:2], 1.0))
            link(dve.reciprocal(silu_c[:, 3:4], silu_c[:, 2:3]))
            link(dve.tensor_tensor(silu_c[:, 1:2], silu_c[:, 0:1], silu_c[:, 3:4], ALU.mult))
            dve.wait_ge(consts, 1)
            dve.tensor_scalar(c_wide[:, :], ones[:, :], silu_c[:, 1:2], None, ALU.mult).then_inc(silu_c_ok, 1)
            dve.wait_ge(x_in, 16)
            statistics(1)
            dve.wait_ge(fill, 1)
            dve.tensor_copy(mods[:, 0:5], aux[:, 0, 0:5])
            dve.tensor_copy(gb_row[:, :], aux[:, 0, P:2 * P]).then_inc(freed, 1)
            dve.wait_ge(freed, 1)
            dve.tensor_scalar_add(mods[:, 1:2], mods[:, 1:2], 1.0)
            dve.tensor_scalar_add(mods[:, 4:5], mods[:, 4:5], 1.0)
            floor_gate(mods[:, 2:3], modt[:, 0:1], modt[:, 1:2])
            floor_gate(gb_row[:, :], gb_tmp[:, 0:D], gb_tmp[:, D:2 * D])
            k = FILLS_MOD
            modulated(k, 0, 1)
            k += FILLS_LN
            dve.memset(y[:, :], 0.0)
            def split(n, c, k, chunks):
                cols = slice(c * BANK, (c + 1) * BANK)
                dve.wait_ge(high_ok, chunks)
                dve.tensor_tensor(qlm[n][0:DH, cols], aux[0:DH, k % RING, :], qhh[n][0:DH, cols].bitcast(F32),
                                  ALU.subtract)
                dve.tensor_tensor(khl[n][DH:P, cols], aux[DH:P, k % RING, :], khl[n][0:DH, cols].bitcast(F32),
                                  ALU.subtract).then_inc(freed, 1)

            def block_max(m, k, moved):
                tile, c = divmod(m, NCHUNK)
                dve.wait_ge(fill, k + moved + 1)
                dve.tensor_reduce(max4[:, tile, c:c + 1], aux[:, k % RING, :], AX_X, ALU.max).then_inc(freed, 1)
                if m == MAX_FILLS - 1:
                    dve.wait_ge(freed, k + moved + 1)
                    dve.tensor_reduce(maxq[:, :], max4[:, :, :], AX_X, ALU.max).then_inc(max_ok, 1)

            def negative_rows(k, moved, heads):
                dve.wait_ge(fill, k + moved + 1)
                if heads is not None:
                    dve.wait_ge(row_in, 16 * heads)
                dve.tensor_scalar(neg_max[:, :], aux[0:KT, k % RING, 0:P], -1.0, None, ALU.mult).then_inc(freed, 1)

            for c in range(NCHUNK):
                split(0, c, k, c + 1)
                k += 1
            for m in range(MAX_FILLS):
                block_max(m, k, 0)
                k += 1
            negative_rows(k, 0, None)

            def add_step(i, half, kt):
                n = len(DVE_KTS) * (4 * i + half) + DVE_KTS.index(kt)
                dve.wait_ge(expd, 128 * i + 32 * half + 2 * kt + 2)
                if kt == DVE_KTS[0]:
                    if not (is_first(i) and half == 0):
                        dve.wait_ge(sums_ok, 4 * i + half)
                    dve.tensor_copy(sum_dve[:, :], probs[:, kt % PT_RING, :]).then_inc(dve_sum, 1)
                else:
                    dve.wait_ge(dve_sum, n)
                    dve.tensor_tensor(sum_dve[:, :], sum_dve[:, :], probs[:, kt % PT_RING, :], ALU.add
                                      ).then_inc(dve_sum, 1)

            def add_pool(halves):
                dve.wait_ge(pool_sum, POOL_PER_HALF * halves)
                dve.wait_ge(dve_sum, len(DVE_KTS) * halves)
                dve.tensor_tensor(sum_dve[:, :], sum_dve[:, :], sum_pool[:, :], ALU.add).then_inc(sums_ok, 1)

            def take_sums(k, moved):
                dve.wait_ge(fill, k + moved + 1)
                dve.tensor_copy(den, aux[:, k % RING, :]).then_inc(freed, 1)

            def divide(halves, half, part, taken):
                odd, f = divmod(half, 2)
                if part < 4:
                    if part == 0:
                        dve.wait_ge(freed, taken)
                    cols = slice(part * P, (part + 1) * P)
                    dve.reciprocal(rden[:, cols], den[:, cols]).then_inc(inverted, 1)
                elif part == 4:
                    dve.wait_ge(inverted, 4 * halves)
                    dve.wait_ge(pv_ok, 16 * halves)
                    lower = 2 * f + 1 if odd else 2 * f
                    dve.tensor_tensor(attn[0:DH, lower, :], out_acc[0:DH, f, :], rden[0:DH, :], ALU.mult)
                else:
                    upper = 2 * f if odd else 2 * f + 1
                    dve.tensor_tensor(attn[DH:P, upper, :], out_acc[DH:P, f, :], rden[DH:P, :], ALU.mult
                                      ).then_inc(normed, 1)

            def add_output(c, k, moved):
                cols = slice(c * BANK, (c + 1) * BANK)
                dve.wait_ge(fill, k + moved + 1)
                dve.tensor_tensor(y[:, cols], y[:, cols], aux[:, k % RING, :], ALU.add).then_inc(freed, 1)

            def body(i):
                k, moved = 0, turn_fills(i)
                for par in range(2):
                    for t in range(STEPS):
                        half, kt = 2 * par + t // KT, t % KT
                        prior = not (is_first(i) and half == 0)
                        if kt - 1 in DVE_KTS:
                            add_step(i, half, kt - 1)
                        if kt == 0 and prior:
                            if half:
                                add_step(i, half - 1, KT - 1)
                            else:
                                add_step(i - 1, 3, KT - 1)
                        if kt == 1 and prior:
                            add_pool(4 * i + half)
                        for what, n in head_work(i, par, t):
                            if what == "project":
                                split(1 - par, n, k, 4 * (2 * i + par + 1) + n + 1)
                            elif what == "sums":
                                take_sums(k, moved)
                                taken = k + moved + 1
                            elif what == "output":
                                add_output(2 * ((half - 1) % 2) + n, k, moved)
                            elif what == "maximum":
                                block_max(n, k, moved)
                            else:
                                negative_rows(k, moved, 2 * i + par + 1)
                            k += 1
                        if prior and 1 <= kt - DEN_AT <= 6:
                            divide(4 * i + half, (half - 1) % 4, kt - DEN_AT - 1, taken)

            pair_loop(dve, body)
            add_step(PAIRS - 1, 3, KT - 1)
            add_pool(4 * PAIRS)
            k = LAST
            take_sums(k, 0)
            for part in range(6):
                divide(4 * PAIRS, 3, part, k + 1)
            for n in range(2):
                add_output(2 + n, k + 1 + n, 0)
            k += 3
            dve.wait_ge(freed, k)
            for q in range(NCHUNK):
                cols = slice(q * BANK, (q + 1) * BANK)
                dve.tensor_scalar(y[:, cols], y[:, cols], mods[:, 2:3], None, ALU.mult).then_inc(tile_ok, 1)
            for q in range(NCHUNK):
                dve.wait_ge(fill, k + 1)
                rows = x[:, 4 * q:4 * q + 4, :].rearrange("p t c -> p (t c)")
                dve.tensor_tensor(rows, rows, aux[:, k % RING, :], ALU.add).then_inc(freed, 1)
                k += 1
            dve.wait_ge(freed, k)
            statistics(2)
            modulated(k, 3, 4)
            k += FILLS_LN
            dve.wait_ge(ffn_in, 64)
            for n in range(E * HH):
                dve.tensor_tensor(w3_sb[:, n, :], w3_raw[:, n, :], gb_row[:, :], ALU.mult)
            dve.wait_ge(fill, k + 1)
            dve.tensor_copy(lg[:, :, :].rearrange("p t e -> p (t e)"), aux[:, k % RING, 0:TT * E]).then_inc(freed, 1)
            dve.wait_ge(freed, k + 1)
            dve.wait_ge(consts, 3 + E)

            def wide(column):
                return column.rearrange("p (t o) -> p t o", o=1).to_broadcast([P, TT, E])

            def choose(logits, top, hot):
                link(dve.tensor_reduce(top, logits, AX_X, ALU.max))
                link(dve.tensor_tensor(key, logits, wide(top), ALU.is_equal))
                link(dve.tensor_tensor(key, key, rank[:, :, :], ALU.mult))
                link(dve.tensor_reduce(pick, key, AX_X, ALU.max))
                link(dve.tensor_tensor(hot, rank[:, :, :], wide(pick), ALU.is_equal))

            choose(lg, top1, hot1)
            link(dve.scalar_tensor_tensor(out=lg2, in0=hot1, scalar=NEVER, in1=lg, op0=ALU.mult, op1=ALU.add))
            choose(lg2, top2, hot2)
            dve.tensor_tensor(dlt, top2, top1, ALU.subtract).then_inc(logits_ok, 1)
            dve.wait_ge(exp_ok, 1)
            link(dve.tensor_scalar_add(dlt, wt2, 1.0))
            link(dve.reciprocal(wt1, dlt))
            link(dve.tensor_tensor(wt2, wt2, wt1, ALU.mult))
            link(dve.tensor_tensor(hot1, hot1, wide(wt1), ALU.mult))
            link(dve.tensor_tensor(hot2, hot2, wide(wt2), ALU.mult))
            dve.tensor_tensor(comb, hot1, hot2, ALU.add).then_inc(weights_ok, 1)
            dve.wait_ge(weights_ok, 1)

            def combine(j):
                if not is_first(j):
                    dve.wait_ge(stored, 16 * j)
                dve.tensor_copy(moe, x[:, bass.ds(4 * j, 4), :]).then_inc(chunk_ok, 1)
                dve.tensor_copy(comb_j, comb[:, bass.ds(4 * j, 4), :]).then_inc(chunk_ok, 1)
                dve.wait_ge(chunk_ok, 2 * j + 2)

                def add_expert(e):
                    dve.wait_ge(down_ok, E * j + e + 1)
                    if not (is_first(j) and e == 0):
                        dve.wait_ge(moe_ok, E * j + e)
                    for t in range(4):
                        ins = dve.scalar_tensor_tensor(out=moe[:, t, :], in0=out_acc[:, e % 2, P * t:P * (t + 1)],
                                                       scalar=comb_j[:, t, e:e + 1], in1=moe[:, t, :],
                                                       op0=ALU.mult, op1=ALU.add)
                    ins.then_inc(moe_ok, 1)

                for b in range(E * HH):
                    e, h = divmod(b, HH)
                    dve.wait_ge(silu_ok, E * HH * j + b + 1)
                    if e >= 2:
                        dve.wait_ge(down_ok, E * j + e - 1)
                    dve.tensor_tensor(up[:, e % 2, h, :], silu_g[:, b % 2, :], aux[:, b % 2, :],
                                      ALU.mult).then_inc(up_ok, 1)
                    if h == HH - 1 and e >= 1:
                        add_expert(e - 1)
                add_expert(E - 1)

            chunk_loop(dve, combine)

        @block.tensor
        def _(pe):
            pe.wait_ge(modulation_in, 32)
            pe.wait_ge(silu_c_ok, 1)
            for n in range(6):
                pe.matmul(aux[:, 0, n:n + 1], wmod[:, n * D:(n + 1) * D], silu_c[:, 1:2], start=True, stop=True)
            pe.matmul(aux[:, 0, P:2 * P], c_wide[:, :], wmod[:, 5 * D:6 * D], start=True, stop=True).then_inc(fill, 1)

            def bank_free(k, moved=0):
                if k >= RING:
                    pe.wait_ge(freed, k + moved - RING + 1)
                elif k == 0:
                    pe.wait_ge(freed, moved)

            def turn_tiles(k, ready, tile):
                for q in range(TT // 4):
                    bank_free(k)
                    for t in range(4):
                        pe.wait_ge(tile_ok, ready(4 * q + t))
                        mm = pe.transpose(aux[:, k % RING, P * t:P * (t + 1)], tile(4 * q + t), ident[:, :])
                    mm.then_inc(fill, 1)
                    k += 1

            pe.wait_ge(consts, 3 + E)
            k = FILLS_MOD
            turn_tiles(k, lambda t: t + 1, lambda t: xn[:, t % 4, :])
            k += FILLS_LN
            pe.wait_ge(w_qkv_in, 16)
            pe.wait_ge(freed, k)
            w_v = w_qkv.rearrange("p (h j d) -> p j h d", j=3, d=DH)[:, 2, :, :]

            def all_v(t, g):
                n = 2 * t + g
                if n >= RING:
                    pe.wait_ge(v_ok, n - RING + 1)
                pe.matmul(score[:, n % RING, :].rearrange("p (h d) -> p h d", d=DH),
                          hT[:, P * t:P * (t + 1)], w_v[:, 8 * g:8 * g + 8, :], start=True, stop=True
                          ).then_inc(v_fill, 1)

            def project(n, c, k, moved):
                bank_free(k, moved)
                pe.matmul(aux[:, k % RING, :], w_head[n][:, :], hT[:, c * BANK:(c + 1) * BANK], start=True, stop=True
                          ).then_inc(fill, 1)

            def query_scores(n, m, k, moved):
                tile, c = divmod(m, NCHUNK)
                bank_free(k, moved)
                if m == 0:
                    pe.wait_ge(freed, k + moved)
                pe.matmul(aux[:, k % RING, :], qhh[n][:, P * tile:P * (tile + 1)], khl[n][:, c * BANK:(c + 1) * BANK],
                          start=True, stop=True).then_inc(fill, 1)

            def turn_maxima(k, moved, heads):
                bank_free(k, moved)
                pe.wait_ge(max_ok, heads)
                pe.transpose(aux[0:KT, k % RING, 0:P], maxq[:, :], ident[:, :]).then_inc(fill, 1)

            pe.wait_ge(w_head_in[0], 16)
            for c in range(NCHUNK):
                project(0, c, k, 0)
                k += 1
            for m in range(MAX_FILLS):
                if m % 2 == 0:
                    all_v(*divmod(m // 2, 2))
                query_scores(0, m, k, 0)
                k += 1
            turn_maxima(k, 0, 1)

            def scores(i, par, t, c):
                f, kt = divmod(t, KT)
                n = 64 * par + 2 * t + c
                keys = slice(P * kt, P * (kt + 1))
                if is_first(i) and n < 2:
                    pe.wait_ge(v_ok, 2 * TT - 1 + n)
                if t == 0 and c == 0:
                    pe.wait_ge(row_in, 16 * (2 * i + par + 1))
                if n >= RING:
                    pe.wait_ge(expd, 128 * i + n - RING + 1)
                elif n < 2 and not is_first(i):
                    pe.wait_ge(expd, 128 * i + n - 1)
                cols = slice(BANK * (2 * f + c), BANK * (2 * f + c + 1))
                o = score[:, n % RING, :]
                pe.matmul(o, khl[par][:, keys], qhh[par][:, cols], start=True, stop=False)
                pe.matmul(o, kh1[par][:, keys], qlm[par][:, cols], start=False, stop=True).then_inc(scored, 1)

            def values(i, par, t):
                f, kt = divmod(t, KT)
                if t == 0:
                    pe.wait_ge(v_in, 16 * (2 * i + par + 1))
                pe.wait_ge(expd, 128 * i + 64 * par + 2 * t + 2)
                if kt == 0 and not (is_first(i) and par == 0):
                    pe.wait_ge(normed, 4 * i + 2 * par + f - 1)
                for c in range(2):
                    mm = pe.matmul(out_acc[DH * c:DH * (c + 1), f, :], v_h[par][:, kt, :],
                                   probs[:, t % PT_RING, BANK * (c ^ par):BANK * ((c ^ par) + 1)],
                                   start=(kt == 0), stop=(kt == KT - 1))
                mm.then_inc(pv_ok, 1)

            def sum_keys(halves, odd, k, moved):
                bank_free(k, moved)
                pe.wait_ge(sums_ok, halves)
                for c in range(2):
                    mm = pe.matmul(aux[DH * c:DH * (c + 1), k % RING, :], ones[:, 0:DH],
                                   sum_dve[:, BANK * (c ^ odd):BANK * ((c ^ odd) + 1)], start=True, stop=True)
                mm.then_inc(fill, 1)

            def project_out(f, n, k, moved, halves, pairs):
                bank_free(k, moved)
                if n == 0:
                    pe.wait_ge(normed, halves)
                    pe.wait_ge(wo_in, 64 * pairs)
                pe.matmul(aux[:, k % RING, :], wo_pair[:, n, :], attn[:, 2 * f + n, :], start=True, stop=True
                          ).then_inc(fill, 1)

            def auxiliary(i, par, t, what, n, k, moved):
                half = 2 * par + t // KT
                if what == "project":
                    if n == 0:
                        pe.wait_ge(w_head_in[1 - par], 16 * (i + par + 1))
                    project(1 - par, n, k, moved)
                elif what == "sums":
                    sum_keys(4 * i + half, ((half - 1) % 4) // 2, k, moved)
                elif what == "output":
                    project_out((half - 1) % 2, n, k, moved, 4 * i + half, i + par)
                elif what == "maximum":
                    query_scores(1 - par, n, k, moved)
                else:
                    turn_maxima(k, moved, 2 * i + par + 2)

            def body(i):
                k, moved = 0, turn_fills(i)
                for par in range(2):
                    for t in range(STEPS):
                        work = head_work(i, par, t)
                        scores(i, par, t, 0)
                        for what, n in work[0:1]:
                            auxiliary(i, par, t, what, n, k, moved)
                        scores(i, par, t, 1)
                        for what, n in work[1:2]:
                            auxiliary(i, par, t, what, n, k + 1, moved)
                        if t > 0:
                            values(i, par, t - 1)
                        elif par == 1:
                            values(i, 0, STEPS - 1)
                        elif not is_first(i):
                            values(i - 1, 1, STEPS - 1)
                        for m, (what, n) in enumerate(work[2:]):
                            auxiliary(i, par, t, what, n, k + 2 + m, moved)
                        k += len(work)

            pair_loop(pe, body)
            values(PAIRS - 1, 1, STEPS - 1)
            k = LAST
            sum_keys(4 * PAIRS, 1, k, 0)
            for n in range(2):
                project_out(1, n, k + 1 + n, 0, 4 * PAIRS, PAIRS)
            k += 3
            turn_tiles(k, lambda t: TT + t // 4 + 1, lambda t: y[:, P * t:P * (t + 1)])
            k += NCHUNK
            turn_tiles(k, lambda t: TT + NCHUNK + t + 1, lambda t: xn[:, t % 4, :])
            k += FILLS_LN
            pe.wait_ge(ffn_in, 64)
            pe.wait_ge(freed, k)
            for t in range(TT):
                mm = pe.matmul(aux[:, k % RING, E * t:E * (t + 1)], hT[:, P * t:P * (t + 1)], wg_sb,
                               start=True, stop=True)
            mm.then_inc(fill, 1)

            pe.wait_ge(freed, k + 1)

            def experts(j):

                def down(e):
                    pe.wait_ge(up_ok, E * HH * j + HH * (e + 1))
                    if e == 0:
                        pe.wait_ge(weights_ok, 1)
                    if not (is_first(j) and e < 2):
                        pe.wait_ge(moe_ok, E * j + e - 1)
                    for t in range(4):
                        for h in range(HH):
                            mm = pe.matmul(out_acc[:, e % 2, P * t:P * (t + 1)], up[:, e % 2, h, P * t:P * (t + 1)],
                                           w3_sb[:, HH * e + h, :], start=(h == 0), stop=(h == HH - 1))
                    mm.then_inc(down_ok, 1)

                for b in range(E * HH):
                    e, h = divmod(b, HH)
                    if not (is_first(j) and b < 2):
                        pe.wait_ge(up_ok, E * HH * j + b - 1)
                    for o, w in ((score, w1_sb), (aux, w2_sb)):
                        mm = pe.matmul(o[:, b % 2, :], w[:, e, P * h:P * (h + 1)],
                                       hT[:, bass.ds(BANK * j, BANK)], start=True, stop=True)
                    mm.then_inc(hg_ok, 1)
                    if h == HH - 1 and e >= 1:
                        down(e - 1)
                down(E - 1)

            chunk_loop(pe, experts)


INPUTS = ["L0_attn_X", "L0_attn_W_qkv", "L0_attn_W_out", "L0_ffn_Wg", "L0_ffn_W1", "L0_ffn_W2", "L0_ffn_W3",
          "L0_c", "L0_wmod"]


def kernel(**inputs):
    import numpy as np
    import concourse.bacc as bacc
    from concourse.bass_utils import run_bass_kernel_spmd

    nc = bacc.Bacc("TRN2", target_bir_lowering=False, num_devices=1)
    arrays, args = {}, []
    for name in INPUTS:
        a = np.asarray(inputs[name])
        if name == "L0_attn_W_qkv":
            a = a.reshape(a.shape[0], HEADS, DH, 3).transpose(0, 1, 3, 2).reshape(a.shape)
        a = np.ascontiguousarray(a)
        arrays[name + "_dram"] = a
        args.append(nc.dram_tensor(name + "_dram", a.shape, mybir.dt.from_np(a.dtype), kind="ExternalInput").ap())
    out = nc.dram_tensor("out_dram", inputs["L0_attn_X"].shape, F32, kind="ExternalOutput").ap()
    layer(nc, *args, out)
    r = run_bass_kernel_spmd(nc, [arrays], core_ids=[0])
    return r.results[0]["out_dram"]
```

```python
from contextlib import ExitStack

import concourse.bass as bass
from concourse import mybir

F32 = mybir.dt.float32
F32R = mybir.dt.float32r
ALU = mybir.AluOpType
ACT = mybir.ActivationFunctionType
AX_X = mybir.AxisListType.X

P = 128
BANK = 512
HEADS = 16
DH = 64
EPS = 1e-5
NEVER = -3.0e38
TOP = 0.25

DVE_KTS = (11, 15)
POOL_ADDS = {kt: max(n, 1) for n, kt in enumerate(kt for kt in range(16) if kt not in DVE_KTS)}
POOL_PER_HALF = max(POOL_ADDS.values())
PT_RING = 4
RING = 3
NCHUNK = 4
KT = 16
STEPS = 2 * KT
DEN_AT = 3
OUT_AT = 11
PROJ_AT = (0, 2, 5, 7)
LAST_OUT_AT = 8
BACK_AT, NORM_AT, TURNED_AT, LOGITS_AT = 25, 28, 29, 30
SPLIT_AT = 12
TURN_AT = 30
MAX_FILLS = 4 * KT
MAX_BLOCKS = (0,) * 9 + (3, 4, 2, 3, 4, 4, 4) + (2, 2, 4, 3, 3, 3, 3, 3, 3, 3, 3, 3, 3, 2, 0, 0)
assert sum(MAX_BLOCKS) == MAX_FILLS and len(MAX_BLOCKS) == STEPS


def aux_work(t, prepare, prior, prior_odd):
    kt = t % KT
    work = []
    if prepare and t in PROJ_AT:
        work.append(("project", PROJ_AT.index(t)))
    if kt == DEN_AT and prior:
        work.append(("sums", 0))
    if kt == OUT_AT and prior and prior_odd:
        work += [("output", 0), ("output", 1)]
    if prepare:
        done = sum(MAX_BLOCKS[:t])
        work += [("maximum", m) for m in range(done, done + MAX_BLOCKS[t])]
    if prepare and t == TURN_AT:
        work.append(("turn", 0))
    return work


def layer(nc, X, W_qkv, W_out, Wg, W1, W2, W3, C, Wmod, out):
    tokens, D = X.shape[1], X.shape[2]
    E, _, HID = W1.shape
    TT = tokens // P
    HH = HID // P
    PAIRS = HEADS // 2
    assert D == P and tokens == NCHUNK * BANK and HEADS * DH == W_out.shape[0] and HH == 2 and TT == KT

    FILLS_MOD, FILLS_LN = 1, TT // 4
    FILLS_PREP = NCHUNK + MAX_FILLS + 1

    def head_work(i, par, t):
        begins = isinstance(i, int) and i == 0
        ends = isinstance(i, int) and i == PAIRS - 1
        half = 2 * par + t // KT
        work = aux_work(t, not (ends and par == 1), not (begins and half == 0), half in (0, 3) and not (ends and half == 3))
        if ends and par == 1:
            work += {KT + LAST_OUT_AT: [("output", 0), ("output", 1)], BACK_AT: [("back", 0), ("back", 1)],
                     TURNED_AT: [("turned", 0), ("turned", 1)], LOGITS_AT: [("logits", 0)]}.get(t, [])
        return work

    FILLS_FIRST = sum(len(head_work(0, par, t)) for par in range(2) for t in range(STEPS))
    FILLS_TURN = sum(len(head_work(1, par, t)) for par in range(2) for t in range(STEPS))
    PROLOGUE = FILLS_MOD + FILLS_LN + FILLS_PREP

    def turn_fills(i):
        if isinstance(i, int) and i == 0:
            return PROLOGUE
        return PROLOGUE + FILLS_FIRST - FILLS_TURN + FILLS_TURN * i

    LAST = turn_fills(PAIRS - 1) + sum(len(head_work(PAIRS - 1, par, t)) for par in range(2) for t in range(STEPS))
    HALF_TILES = TT // 2

    ctx = ExitStack()
    with ctx:
        def sb(name, shape, dt=F32):
            return ctx.enter_context(nc.sbuf_tensor(name, shape, dt))

        def sem(name):
            return ctx.enter_context(nc.semaphore(name))

        x = sb("x", [P, TT, D])
        hT = sb("hT", [P, tokens])
        khl = [sb(f"khl{n}", [P, tokens], F32R) for n in range(2)]
        kh1 = [sb(f"kh1{n}", [DH + 1, tokens], F32R) for n in range(2)]
        qhh = [sb(f"qhh{n}", [P, tokens], F32R) for n in range(2)]
        qlm = [sb(f"qlm{n}", [DH + 1, tokens], F32R) for n in range(2)]
        v_h = [sb(f"v_h{n}", [P, KT, DH]) for n in range(2)]
        probs = sb("probs", [P, PT_RING, 2 * BANK])
        w_qkv = probs[:, 0:3, :].rearrange("p a b -> p (a b)")
        sum_pool = sb("sum_pool", [P, 2 * BANK])
        sum_dve = sb("sum_dve", [P, 2 * BANK])
        attn = sb("attn", [P, NCHUNK, BANK])
        y = sb("y", [P, tokens])
        rden = sb("rden", [P, BANK])
        w_head = [sb(f"w_head{n}", [P, 2 * DH]) for n in range(2)]
        wo_pair = sb("wo_pair", [P, 2, D])
        wmod = sb("wmod", [P, 6 * D])
        den = wmod[:, 0:BANK]
        ident = sb("ident", [P, P])
        ones = sb("ones", [P, P])
        silu_c = sb("silu_c", [P, 4])
        c_wide = sb("c_wide", [P, P])
        mods = sb("mods", [P, 8])
        modt = sb("modt", [P, 8])
        gb_row = sb("gb_row", [P, D])
        gb_tmp = sb("gb_tmp", [P, 2 * D])
        rank = sb("rank", [P, TT, E])
        stats = sb("stats", [P, TT, 6])
        mv = sb("mv", [P, TT, 2])
        rstd, var, std = sb("rstd", [P, TT]), sb("var", [P, TT]), sb("std", [P, TT])
        xn = sb("xn", [P, 4, D])
        max4 = sb("max4", [P, KT, NCHUNK])
        maxq = sb("maxq", [P, KT])
        neg_max = sb("neg_max", [KT, P], F32R)

        score = ctx.enter_context(nc.psum_tensor("score", [P, RING, BANK], F32))
        out_acc = ctx.enter_context(nc.psum_tensor("out_acc", [P, 2, BANK], F32))
        aux = ctx.enter_context(nc.psum_tensor("aux", [P, RING, BANK], F32))

        with nc.sbuf_tensor("v_all", [P, HEADS, KT * DH], F32) as v_all:
            pass
        with nc.sbuf_tensor("w1_w2", [P, 2, E, HID], F32) as w1_w2:
            pass
        h_high, h_low = sb("h_high", [P, tokens], F32R), sb("h_low", [P, tokens], F32R)
        w_lows = [sb(f"w_low{n}", [P, E * HID], F32R) for n in range(2)]
        w_highs = [khl[0], qhh[0]]
        w3_sb = sb("w3", [P, E * HH, D])[:, :, :]
        up = sb("up", [P, 2, HH, BANK])
        silu_g = sb("silu_g", [P, 2, BANK])
        moe = sb("moe", [P, 4, D])[:, :, :]
        wg_sb = sb("wg", [P, E])[:, :]
        lg, lg2, key, hot1, hot2, comb = (sb(name, [P, TT, E]) for name in ("lg", "lg2", "key", "hot1", "hot2", "comb"))
        comb_j = sb("comb_j", [P, 4, E])[:, :, :]
        top1, top2, pick, dlt, wt1, wt2 = (sb(name, [P, TT]) for name in ("top1", "top2", "pick", "dlt", "wt1", "wt2"))
        xn2 = sb("xn2", [P, TT // 2, D])

        def ring_fill(k, moved):
            return aux[:, k % RING, :], k + moved - RING + 1 if k >= RING else moved, k + moved + 1

        def late_fill(k):
            return (aux, score)[k % 2][:, 2, :], LAST + max(k - 1, 0), LAST + k + 1

        modulation_in, x_in, w_qkv_in = sem("modulation_in"), sem("x_in"), sem("w_qkv_in")
        w_head_in = [sem("w_head_in0"), sem("w_head_in1")]
        v_in, wo_in, row_in, ffn_in = sem("v_in"), sem("wo_in"), sem("row_in"), sem("ffn_in")
        consts = sem("consts")
        exp_c = sem("exp_c")
        silu_c_ok = sem("silu_c_ok")
        var_ok = sem("var_ok")
        std_ok = sem("std_ok")
        tile_ok = sem("tile_ok")
        fill = sem("fill")
        freed = sem("freed")
        v_fill = sem("v_fill")
        v_ok = sem("v_ok")
        high_ok = sem("high_ok")
        max_ok = sem("max_ok")
        scored = sem("scored")
        expd = sem("expd")
        pv_ok = sem("pv_ok")
        pool_sum = sem("pool_sum")
        dve_sum = sem("dve_sum")
        sums_ok = sem("sums_ok")
        inverted = sem("inverted")
        normed = sem("normed")
        logits_ok = sem("logits_ok")
        exp_ok = sem("exp_ok")
        weights_ok = sem("weights_ok")
        chunk_ok = sem("chunk_ok")
        hg_ok = sem("hg_ok")
        silu_ok = sem("silu_ok")
        up_ok = sem("up_ok")
        w_high_ok = sem("w_high_ok")
        w_low_ok = sem("w_low_ok")
        h_high_ok = sem("h_high_ok")
        h_low_ok = sem("h_low_ok")
        down_ok = sem("down_ok")
        moe_ok = sem("moe_ok")
        stored = sem("stored")
        dve_did = sem("dve_did")

        block = ctx.enter_context(nc.Block())
        wo_rows = W_out.rearrange("(a d) c -> a d c", d=DH)

        def pair_loop(eng, body):
            body(0)
            with eng.Fori(1, PAIRS - 1) as i:
                body(i)
            body(PAIRS - 1)

        def chunk_loop(eng, body):
            body(0)
            body(1)
            with eng.Fori(2, NCHUNK) as j:
                body(j)

        def is_number(j, block_number, n):
            return isinstance(j, int) and block_number == n

        def is_first(i):
            return isinstance(i, int) and i == 0

        def is_last(i):
            return isinstance(i, int) and i == PAIRS - 1

        @block.sync
        def _(sp):
            sp.dma_start(silu_c[:, 0:1], C.rearrange("a d -> d a")).then_inc(modulation_in, 16)
            sp.dma_start(wmod[:, :], Wmod).then_inc(modulation_in, 16)
            sp.dma_start(x[:, :, :], X[0].rearrange("(t p) c -> p t c", p=P)).then_inc(x_in, 16)
            sp.dma_start(w_qkv, W_qkv).then_inc(w_qkv_in, 16)
            for n in range(2):
                sp.dma_start(w_head[n][:, :], W_qkv[:, 3 * DH * n:3 * DH * n + 2 * DH]).then_inc(w_head_in[n], 16)

            def max_row(n):
                sp.dma_start(qlm[n][DH:DH + 1, :].bitcast(F32), neg_max[:, :].bitcast(F32)
                             ).then_inc(row_in, 16)

            sp.wait_ge(v_ok, 2 * TT)
            sp.dma_start(v_h[0][:, :, :].rearrange("p k d -> p (k d)"), v_all[:, 0, :]).then_inc(v_in, 16)
            sp.wait_ge(freed, PROLOGUE)
            max_row(0)

            def body(i):
                k, moved = 0, turn_fills(i)
                for par in range(2):
                    nxt = 1 - par
                    if not is_last(i):
                        sp.wait_ge(freed, k + moved)
                        sp.dma_start(w_head[par][:, :], W_qkv[:, bass.ds(6 * DH * i + 3 * DH * (par + 2), 2 * DH)]
                                     ).then_inc(w_head_in[par], 16)
                    if not (is_last(i) and par == 1):
                        if not (is_first(i) and par == 0):
                            sp.wait_ge(pv_ok, 64 * i + 32 * par)
                        sp.dma_start(v_h[nxt][:, :, :].rearrange("p k d -> p (k d)"),
                                     v_all[:, bass.ds(2 * i + par + 1, 1), :].rearrange("p a n -> p (a n)")
                                     ).then_inc(v_in, 16)
                    for t in range(STEPS):
                        k += len(head_work(i, par, t))
                        if par == 0 and t == OUT_AT:
                            sp.wait_ge(freed, k + moved)
                            for s in range(2):
                                for n in range(2):
                                    sp.dma_start(wo_pair[DH * n:DH * (n + 1), s, :],
                                                 wo_rows[bass.ds(2 * i + (n ^ s), 1), :, :]
                                                 .rearrange("a d c -> (a d) c")).then_inc(wo_in, 16)
                    if not (is_last(i) and par == 1):
                        sp.wait_ge(freed, k + moved)
                        max_row(nxt)

            pair_loop(sp, body)
            sp.wait_ge(v_in, 16 * HEADS)
            sp.dma_start(wg_sb, Wg).then_inc(ffn_in, 16)
            sp.dma_start(w1_w2[:, 0, :, :], W1.rearrange("e c n -> c e n")).then_inc(ffn_in, 16)
            sp.dma_start(w1_w2[:, 1, :, :], W2.rearrange("e c n -> c e n")).then_inc(ffn_in, 16)
            sp.dma_start(w3_sb, W3.rearrange("e (h p) c -> p (e h) c", p=P)).then_inc(ffn_in, 16)
            out_chunks = out[0].rearrange("(j t p) c -> j p t c", p=P, t=4)

            def store(j):
                sp.wait_ge(moe_ok, E * j + E)
                sp.dma_start(out_chunks[bass.ds(j, 1), :, :, :].rearrange("j p t c -> (j p) t c"), moe
                             ).then_inc(stored, 16)

            chunk_loop(sp, store)
            sp.wait_ge(stored, 16 * NCHUNK)

        @block.gpsimd
        def _(pool):
            pool.memset(ones[:, :], 1.0).then_inc(consts, 1)
            pool.memset(ident[:, :], 0.0).then_inc(consts, 1)
            for e in range(E):
                pool.memset(rank[:, :, e], float(E - e)).then_inc(consts, 1)
            pool.wait_ge(consts, 2)
            pool.affine_select(out=ident[:, :], in_=ident[:, :], compare_op=ALU.not_equal, fill=1.0, base=0,
                               pattern=[[-1, P]], channel_multiplier=1).then_inc(consts, 1)

            def body(i):
                for half in range(4):
                    done = POOL_PER_HALF * (4 * i + half)
                    for kt in sorted(POOL_ADDS)[1:]:
                        pool.wait_ge(expd, 128 * i + 32 * half + 2 * kt + 2)
                        if not (is_first(i) and half == 0 and kt == 1):
                            pool.wait_ge(pool_sum, done + POOL_ADDS[kt] - 1)
                        if kt > 1:
                            pool.tensor_tensor(sum_pool[:, :], sum_pool[:, :], probs[:, kt % PT_RING, :], ALU.add
                                               ).then_inc(pool_sum, 1)
                            continue
                        if not (is_first(i) and half == 0):
                            pool.wait_ge(sums_ok, 4 * i + half)
                        pool.tensor_tensor(sum_pool[:, :], probs[:, 0, :], probs[:, 1, :], ALU.add
                                           ).then_inc(pool_sum, 1)

            pair_loop(pool, body)

        @block.scalar
        def _(act):
            act.wait_ge(modulation_in, 32)
            act.activation(silu_c[:, 1:2], silu_c[:, 0:1], ACT.Exp, scale=-1.0).then_inc(exp_c, 1)
            act.wait_ge(var_ok, 1)
            act.sqrt(std[:, :], var[:, :]).then_inc(std_ok, 1)

            def high_parts(n, c, k, moved):
                cols = slice(c * BANK, (c + 1) * BANK)
                act.wait_ge(fill, k + moved + 1)
                act.copy(qhh[n][0:DH, cols], aux[0:DH, k % RING, :])
                act.copy(qhh[n][DH:P, cols], aux[0:DH, k % RING, :])
                act.copy(kh1[n][0:DH, cols], aux[DH:P, k % RING, :])
                act.copy(khl[n][0:DH, cols], aux[DH:P, k % RING, :]).then_inc(high_ok, 1)

            for c in range(NCHUNK):
                high_parts(0, c, FILLS_MOD + FILLS_LN + c, 0)
            for n in range(2 * TT):
                t, g = divmod(n, 2)
                act.wait_ge(v_fill, n + 1)
                act.copy(v_all[:, 8 * g:8 * g + 8, DH * t:DH * (t + 1)],
                         score[:, n % RING, :].rearrange("p (h d) -> p h d", d=DH)).then_inc(v_ok, 1)

            def slot_free(i, half, kt):
                if is_first(i) and half == 0 and kt < PT_RING:
                    return
                act.wait_ge(pv_ok, 64 * i + 16 * half + kt - PT_RING + 1)
                old, before = (kt - PT_RING, 4 * i + half) if kt >= PT_RING else (kt - PT_RING + KT, 4 * i + half - 1)
                if old in POOL_ADDS:
                    act.wait_ge(pool_sum, POOL_PER_HALF * before + POOL_ADDS[old])
                else:
                    act.wait_ge(dve_sum, len(DVE_KTS) * before + DVE_KTS.index(old) + 1)

            def body(i):
                k, moved = 0, turn_fills(i)
                for par in range(2):
                    for t in range(STEPS):
                        for c in range(2):
                            act.wait_ge(scored, 128 * i + 64 * par + 2 * t + c + 1)
                            if c == 0:
                                slot_free(i, 2 * par + t // KT, t % KT)
                            act.activation(probs[:, t % PT_RING, BANK * c:BANK * (c + 1)],
                                           score[:, (par + 2 * t + c) % RING, :], ACT.Exp, scale=DH ** -0.5
                                           ).then_inc(expd, 1)
                        for what, n in head_work(i, par, t):
                            if what == "project":
                                high_parts(1 - par, n, k, moved)
                            k += 1
                        if is_last(i) and par == 1:
                            if 0 <= t - SPLIT_AT < 2 * NCHUNK:
                                weights_high(t - SPLIT_AT)
                            if t == NORM_AT - 1:
                                root(0)
                            if t == TURNED_AT + 1:
                                for c in range(2):
                                    tokens_high(c, moved + turned_fills + c)
                            if t == TURNED_AT:
                                turned_fills = k - 1

            def weights_high(n):
                cols = slice(BANK * (n % 4), BANK * (n % 4 + 1))
                act.wait_ge(ffn_in, 64)
                whole = w1_w2[:, n // 4, :, :].rearrange("p e n -> p (e n)")
                act.copy(w_highs[n // 4][:, cols], whole[:, cols]).then_inc(w_high_ok, 1)

            def tokens_high(c, done):
                cols = slice(BANK * c, BANK * (c + 1))
                act.wait_ge(freed, done)
                act.copy(h_high[:, cols], hT[:, cols]).then_inc(h_high_ok, 1)

            def root(f):
                tiles = slice(HALF_TILES * f, HALF_TILES * (f + 1))
                act.wait_ge(var_ok, 2 + f)
                act.sqrt(std[:, tiles], var[:, tiles]).then_inc(std_ok, 1)

            def exp_logits(f):
                tiles = slice(HALF_TILES * f, HALF_TILES * (f + 1))
                act.wait_ge(logits_ok, 1 + f)
                act.activation(wt2[:, tiles], dlt[:, tiles], ACT.Exp).then_inc(exp_ok, 1)

            pair_loop(act, body)
            exp_logits(0)

            def gates(j):
                for b in range(E * HH):
                    act.wait_ge(hg_ok, E * HH * j + b + 1)
                    if not (is_first(j) and b < 2):
                        act.wait_ge(up_ok, E * HH * j + b - 1)
                    act.activation(silu_g[:, b % 2, :], score[:, b % 2, :], ACT.Silu).then_inc(silu_ok, 1)
                    if is_number(j, E * HH * j + b, 15):
                        root(1)
                    for c in range(2):
                        if is_number(j, E * HH * j + b, 20 + c):
                            tokens_high(2 + c, LAST + 6 + c)
                    if is_number(j, E * HH * j + b, 24):
                        exp_logits(1)

            chunk_loop(act, gates)

        @block.vector
        def _(dve):
            did = [0]

            def link(ins):
                did[0] += 1
                ins.then_inc(dve_did, 1)
                dve.wait_ge(dve_did, did[0])

            def normalise(t, to):
                dve.tensor_scalar(to, x[:, t, :], mv[:, t, 0:1], rstd[:, t:t + 1],
                                  ALU.subtract, ALU.mult).then_inc(tile_ok, 1)

            def variances(t0, t1):
                for t in range(t0, t1 - 1):
                    dve.bn_stats(stats[:, t, :], x[:, t, :])
                link(dve.bn_stats(stats[:, t1 - 1, :], x[:, t1 - 1, :]))
                for t in range(t0, t1 - 1):
                    dve.bn_aggr(mv[:, t, :], stats[:, t, :])
                link(dve.bn_aggr(mv[:, t1 - 1, :], stats[:, t1 - 1, :]))
                dve.tensor_scalar_add(var[:, t0:t1], mv[:, t0:t1, 1], EPS).then_inc(var_ok, 1)

            def inverse_roots(t0, t1, n):
                r, s, v = (a[:, t0:t1] for a in (rstd, std, var))
                dve.wait_ge(std_ok, n)
                link(dve.reciprocal(r, s))
                link(dve.tensor_tensor(s, r, r, ALU.mult))
                link(dve.tensor_tensor(s, s, v, ALU.mult))
                link(dve.tensor_scalar(s, s, -0.5, 1.5, ALU.mult, ALU.add))
                link(dve.tensor_tensor(r, r, s, ALU.mult))

            def modulate(c, place, shift, scale):
                bank, _, filled = place
                dve.wait_ge(fill, filled)
                dve.tensor_scalar(hT[:, c * BANK:(c + 1) * BANK], bank, mods[:, scale:scale + 1],
                                  mods[:, shift:shift + 1], ALU.mult, ALU.add).then_inc(freed, 1)

            def floor_gate(gate, tmp, size):
                link(dve.scalar_tensor_tensor(out=size, in0=gate, scalar=-1.0, in1=gate, op0=ALU.mult, op1=ALU.max))
                link(dve.tensor_scalar(tmp, gate, 0.0, 2.0, ALU.is_ge, ALU.mult))
                link(dve.tensor_scalar(size, size, TOP, None, ALU.max))
                link(dve.scalar_tensor_tensor(out=gate, in0=tmp, scalar=-1.0, in1=size, op0=ALU.add, op1=ALU.mult))

            for n in range(2):
                dve.memset(kh1[n][DH:DH + 1, :].bitcast(F32), 1.0)
            dve.wait_ge(exp_c, 1)
            link(dve.tensor_scalar_add(silu_c[:, 2:3], silu_c[:, 1:2], 1.0))
            link(dve.reciprocal(silu_c[:, 3:4], silu_c[:, 2:3]))
            link(dve.tensor_tensor(silu_c[:, 1:2], silu_c[:, 0:1], silu_c[:, 3:4], ALU.mult))
            dve.wait_ge(consts, 1)
            dve.tensor_scalar(c_wide[:, :], ones[:, :], silu_c[:, 1:2], None, ALU.mult).then_inc(silu_c_ok, 1)
            dve.wait_ge(x_in, 16)
            variances(0, TT)
            inverse_roots(0, TT, 1)
            for t in range(4):
                normalise(t, xn[:, t, :])
            dve.wait_ge(fill, 1)
            dve.tensor_copy(mods[:, 0:5], aux[:, 0, 0:5])
            dve.tensor_copy(gb_row[:, :], aux[:, 0, P:2 * P]).then_inc(freed, 1)
            dve.wait_ge(freed, 1)
            dve.tensor_scalar_add(mods[:, 1:2], mods[:, 1:2], 1.0)
            dve.tensor_scalar_add(mods[:, 4:5], mods[:, 4:5], 1.0)
            floor_gate(mods[:, 2:3], modt[:, 0:1], modt[:, 1:2])
            floor_gate(gb_row[:, :], gb_tmp[:, 0:D], gb_tmp[:, D:2 * D])
            k = FILLS_MOD
            for q in range(NCHUNK):
                modulate(q, ring_fill(k + q, 0), 0, 1)
                for t in range(4 * (q + 1), min(4 * (q + 2), TT)):
                    normalise(t, xn[:, t % 4, :])
            k += FILLS_LN
            dve.memset(y[:, :], 0.0)
            def split(n, c, k, chunks):
                cols = slice(c * BANK, (c + 1) * BANK)
                dve.wait_ge(high_ok, chunks)
                dve.tensor_tensor(qlm[n][0:DH, cols], aux[0:DH, k % RING, :], qhh[n][0:DH, cols].bitcast(F32),
                                  ALU.subtract)
                dve.tensor_tensor(khl[n][DH:P, cols], aux[DH:P, k % RING, :], khl[n][0:DH, cols].bitcast(F32),
                                  ALU.subtract).then_inc(freed, 1)

            def block_max(m, k, moved):
                tile, c = divmod(m, NCHUNK)
                dve.wait_ge(fill, k + moved + 1)
                dve.tensor_reduce(max4[:, tile, c:c + 1], aux[:, k % RING, :], AX_X, ALU.max).then_inc(freed, 1)
                if m == MAX_FILLS - 1:
                    dve.wait_ge(freed, k + moved + 1)
                    dve.tensor_reduce(maxq[:, :], max4[:, :, :], AX_X, ALU.max).then_inc(max_ok, 1)

            def negative_rows(k, moved, heads):
                dve.wait_ge(fill, k + moved + 1)
                if heads is not None:
                    dve.wait_ge(row_in, 16 * heads)
                dve.tensor_scalar(neg_max[:, :], aux[0:KT, k % RING, 0:P], -1.0, None, ALU.mult).then_inc(freed, 1)

            for c in range(NCHUNK):
                split(0, c, k, c + 1)
                k += 1
            for m in range(MAX_FILLS):
                block_max(m, k, 0)
                k += 1
            negative_rows(k, 0, None)

            def add_step(i, half, kt):
                n = len(DVE_KTS) * (4 * i + half) + DVE_KTS.index(kt)
                dve.wait_ge(expd, 128 * i + 32 * half + 2 * kt + 2)
                if kt == DVE_KTS[0]:
                    if not (is_first(i) and half == 0):
                        dve.wait_ge(sums_ok, 4 * i + half)
                    dve.tensor_copy(sum_dve[:, :], probs[:, kt % PT_RING, :]).then_inc(dve_sum, 1)
                else:
                    dve.wait_ge(dve_sum, n)
                    dve.tensor_tensor(sum_dve[:, :], sum_dve[:, :], probs[:, kt % PT_RING, :], ALU.add
                                      ).then_inc(dve_sum, 1)

            def add_pool(halves):
                dve.wait_ge(pool_sum, POOL_PER_HALF * halves)
                dve.wait_ge(dve_sum, len(DVE_KTS) * halves)
                dve.tensor_tensor(sum_dve[:, :], sum_dve[:, :], sum_pool[:, :], ALU.add).then_inc(sums_ok, 1)

            def take_sums(place):
                bank, _, filled = place
                dve.wait_ge(fill, filled)
                dve.tensor_copy(den, bank).then_inc(freed, 1)

            def divide(halves, half, part, taken):
                odd, f = divmod(half, 2)
                if part < 4:
                    if part == 0:
                        dve.wait_ge(freed, taken)
                    cols = slice(part * P, (part + 1) * P)
                    dve.reciprocal(rden[:, cols], den[:, cols]).then_inc(inverted, 1)
                elif part == 4:
                    dve.wait_ge(inverted, 4 * halves)
                    dve.wait_ge(pv_ok, 16 * halves)
                    lower = 2 * f + 1 if odd else 2 * f
                    dve.tensor_tensor(attn[0:DH, lower, :], out_acc[0:DH, f, :], rden[0:DH, :], ALU.mult)
                else:
                    upper = 2 * f if odd else 2 * f + 1
                    dve.tensor_tensor(attn[DH:P, upper, :], out_acc[DH:P, f, :], rden[DH:P, :], ALU.mult
                                      ).then_inc(normed, 1)

            def add_output(c, place):
                bank, _, filled = place
                cols = slice(c * BANK, (c + 1) * BANK)
                dve.wait_ge(fill, filled)
                dve.tensor_tensor(y[:, cols], y[:, cols], bank, ALU.add).then_inc(freed, 1)

            def gate_output(f, done):
                dve.wait_ge(freed, done)
                for c in (2 * f, 2 * f + 1):
                    cols = slice(c * BANK, (c + 1) * BANK)
                    dve.tensor_scalar(y[:, cols], y[:, cols], mods[:, 2:3], None, ALU.mult).then_inc(tile_ok, 1)

            def residual(c, place):
                bank, _, filled = place
                dve.wait_ge(fill, filled)
                rows = x[:, 4 * c:4 * c + 4, :].rearrange("p t c -> p (t c)")
                dve.tensor_tensor(rows, rows, bank, ALU.add).then_inc(freed, 1)

            def second_variances(f, done):
                dve.wait_ge(freed, done)
                variances(HALF_TILES * f, HALF_TILES * (f + 1))

            def second_norm(f, n0, n1):
                if n0 == 0:
                    inverse_roots(HALF_TILES * f, HALF_TILES * (f + 1), 2 + f)
                for n in range(n0, n1):
                    normalise(HALF_TILES * f + n, xn2[:, n, :])

            def weights_low(n):
                cols = slice(BANK * (n % 4), BANK * (n % 4 + 1))
                dve.wait_ge(w_high_ok, n + 1)
                whole = w1_w2[:, n // 4, :, :].rearrange("p e n -> p (e n)")
                dve.tensor_tensor(w_lows[n // 4][:, cols], whole[:, cols], w_highs[n // 4][:, cols].bitcast(F32), ALU.subtract
                                  ).then_inc(w_low_ok, 1)

            def tokens_low(c):
                cols = slice(BANK * c, BANK * (c + 1))
                dve.wait_ge(h_high_ok, c + 1)
                dve.tensor_tensor(h_low[:, cols], hT[:, cols], h_high[:, cols].bitcast(F32), ALU.subtract
                                  ).then_inc(h_low_ok, 1)

            def scale_w3():
                dve.wait_ge(ffn_in, 64)
                dve.tensor_tensor(w3_sb, w3_sb, gb_row[:, :].rearrange("p (o n) -> p o n", o=1)
                                  .to_broadcast([P, E * HH, D]), ALU.mult).then_inc(weights_ok, 1)

            def wide(column):
                return column.rearrange("p (t o) -> p t o", o=1).to_broadcast([P, HALF_TILES, E])

            def choose(f, logits, top, hot):
                tiles = slice(HALF_TILES * f, HALF_TILES * (f + 1))
                link(dve.tensor_reduce(top[:, tiles], logits[:, tiles, :], AX_X, ALU.max))
                link(dve.tensor_tensor(key[:, tiles, :], logits[:, tiles, :], wide(top[:, tiles]), ALU.is_equal))
                link(dve.tensor_tensor(key[:, tiles, :], key[:, tiles, :], rank[:, tiles, :], ALU.mult))
                link(dve.tensor_reduce(pick[:, tiles], key[:, tiles, :], AX_X, ALU.max))
                link(dve.tensor_tensor(hot[:, tiles, :], rank[:, tiles, :], wide(pick[:, tiles]), ALU.is_equal))

            def choose_first(f, place):
                bank, _, filled = place
                tiles = slice(HALF_TILES * f, HALF_TILES * (f + 1))
                dve.wait_ge(fill, filled)
                dve.tensor_copy(lg[:, tiles, :].rearrange("p t e -> p (t e)"), bank[:, 0:HALF_TILES * E]
                                ).then_inc(freed, 1)
                dve.wait_ge(freed, filled)
                dve.wait_ge(consts, 3 + E)
                choose(f, lg, top1, hot1)

            def choose_second(f):
                tiles = slice(HALF_TILES * f, HALF_TILES * (f + 1))
                link(dve.scalar_tensor_tensor(out=lg2[:, tiles, :], in0=hot1[:, tiles, :], scalar=NEVER,
                                              in1=lg[:, tiles, :], op0=ALU.mult, op1=ALU.add))
                choose(f, lg2, top2, hot2)
                dve.tensor_tensor(dlt[:, tiles], top2[:, tiles], top1[:, tiles], ALU.subtract).then_inc(logits_ok, 1)

            def expert_weights(f):
                tiles = slice(HALF_TILES * f, HALF_TILES * (f + 1))
                w1, w2, d = wt1[:, tiles], wt2[:, tiles], dlt[:, tiles]
                h1, h2 = hot1[:, tiles, :], hot2[:, tiles, :]
                dve.wait_ge(exp_ok, 1 + f)
                link(dve.tensor_scalar_add(d, w2, 1.0))
                link(dve.reciprocal(w1, d))
                link(dve.tensor_tensor(w2, w2, w1, ALU.mult))
                link(dve.tensor_tensor(h1, h1, wide(w1), ALU.mult))
                link(dve.tensor_tensor(h2, h2, wide(w2), ALU.mult))
                dve.tensor_tensor(comb[:, tiles, :], h1, h2, ALU.add).then_inc(weights_ok, 1)

            def body(i):
                k, moved = 0, turn_fills(i)
                for par in range(2):
                    for t in range(STEPS):
                        half, kt = 2 * par + t // KT, t % KT
                        prior = not (is_first(i) and half == 0)
                        if kt - 1 in DVE_KTS:
                            add_step(i, half, kt - 1)
                        if kt == 0 and prior:
                            if half:
                                add_step(i, half - 1, KT - 1)
                            else:
                                add_step(i - 1, 3, KT - 1)
                        if kt == 1 and prior:
                            add_pool(4 * i + half)
                        for what, n in head_work(i, par, t):
                            if what == "project":
                                split(1 - par, n, k, 4 * (2 * i + par + 1) + n + 1)
                            elif what == "sums":
                                take_sums(ring_fill(k, moved))
                                taken = k + moved + 1
                            elif what == "output":
                                add_output(2 * ((half - 1) % 2) + n, ring_fill(k, moved))
                            elif what == "maximum":
                                block_max(n, k, moved)
                            elif what == "turn":
                                negative_rows(k, moved, 2 * i + par + 1)
                            elif what == "back":
                                residual(n, ring_fill(k, moved))
                            elif what == "turned":
                                modulate(n, ring_fill(k, moved), 3, 4)
                            else:
                                choose_first(0, ring_fill(k, moved))
                                choose_second(0)
                            k += 1
                        if prior and not (is_last(i) and half == 3) and 1 <= kt - DEN_AT <= 6:
                            divide(4 * i + half, (half - 1) % 4, kt - DEN_AT - 1, taken)
                        if is_last(i) and half == 2 and 0 <= t - SPLIT_AT - 1 < 2 * NCHUNK:
                            weights_low(t - SPLIT_AT - 1)
                        if not (is_last(i) and half == 3):
                            continue
                        if 1 <= kt - DEN_AT <= 3:
                            for part in range(2):
                                divide(4 * i + half, half - 1, 2 * (kt - DEN_AT - 1) + part, taken)
                        if 0 <= t - SPLIT_AT - 1 < 2 * NCHUNK:
                            weights_low(t - SPLIT_AT - 1)
                        if kt == LAST_OUT_AT - 1:
                            scale_w3()
                        if kt == LAST_OUT_AT:
                            gate_output(0, k + moved)
                        if t == BACK_AT:
                            second_variances(0, k + moved)
                        if t == NORM_AT:
                            second_norm(0, 0, HALF_TILES)
                        if t == STEPS - 1:
                            for c in range(2):
                                tokens_low(c)

            pair_loop(dve, body)
            expert_weights(0)

            def late(n):
                if n == 0:
                    add_step(PAIRS - 1, 3, KT - 1)
                elif n == 1:
                    add_pool(4 * PAIRS)
                elif n == 3:
                    take_sums(late_fill(0))
                    for part in (0, 1):
                        divide(4 * PAIRS, 3, part, LAST + 1)
                elif n in (4, 5):
                    for part in (2 * n - 6, 2 * n - 5):
                        divide(4 * PAIRS, 3, part, LAST + 1)
                elif n == 9:
                    for c in range(2):
                        add_output(2 + c, late_fill(1 + c))
                elif n == 10:
                    gate_output(1, LAST + 3)
                elif n == 12:
                    for c in range(2):
                        residual(2 + c, late_fill(3 + c))
                elif n == 14:
                    second_variances(1, LAST + 5)
                elif n == 16:
                    second_norm(1, 0, 4)
                elif n == 17:
                    second_norm(1, 4, HALF_TILES)
                elif n in (19, 20):
                    modulate(2 + n - 19, late_fill(5 + n - 19), 3, 4)
                elif n == 22:
                    choose_first(1, late_fill(7))
                elif n == 23:
                    choose_second(1)
                elif n == 24:
                    for c in range(2):
                        tokens_low(2 + c)
                elif n == 25:
                    expert_weights(1)

            def combine(j):

                def begin():
                    if not is_first(j):
                        dve.wait_ge(stored, 16 * j)
                    dve.wait_ge(weights_ok, 2 if isinstance(j, int) else 3)
                    dve.tensor_copy(moe, x[:, bass.ds(4 * j, 4), :]).then_inc(chunk_ok, 1)
                    dve.tensor_copy(comb_j, comb[:, bass.ds(4 * j, 4), :]).then_inc(chunk_ok, 1)
                    dve.wait_ge(chunk_ok, 2 * j + 2)

                def add_expert(e):
                    dve.wait_ge(down_ok, E * j + e + 1)
                    if not (is_first(j) and e == 0):
                        dve.wait_ge(moe_ok, E * j + e)
                    for t in range(4):
                        ins = dve.scalar_tensor_tensor(out=moe[:, t, :], in0=out_acc[:, e % 2, P * t:P * (t + 1)],
                                                       scalar=comb_j[:, t, e:e + 1], in1=moe[:, t, :],
                                                       op0=ALU.mult, op1=ALU.add)
                    ins.then_inc(moe_ok, 1)

                for b in range(E * HH):
                    e, h = divmod(b, HH)
                    dve.wait_ge(silu_ok, E * HH * j + b + 1)
                    if e >= 2:
                        dve.wait_ge(down_ok, E * j + e - 1)
                    dve.tensor_tensor(up[:, e % 2, h, :], silu_g[:, b % 2, :], aux[:, b % 2, :],
                                      ALU.mult).then_inc(up_ok, 1)
                    if b == 2:
                        begin()
                    if isinstance(j, int):
                        late(E * HH * j + b)
                    if h == HH - 1 and e >= 1:
                        add_expert(e - 1)
                add_expert(E - 1)

            chunk_loop(dve, combine)

        @block.tensor
        def _(pe):
            pe.wait_ge(modulation_in, 32)
            pe.wait_ge(silu_c_ok, 1)
            for n in range(6):
                pe.matmul(aux[:, 0, n:n + 1], wmod[:, n * D:(n + 1) * D], silu_c[:, 1:2], start=True, stop=True)
            pe.matmul(aux[:, 0, P:2 * P], c_wide[:, :], wmod[:, 5 * D:6 * D], start=True, stop=True).then_inc(fill, 1)

            def bank_free(k, moved=0):
                if k >= RING:
                    pe.wait_ge(freed, k + moved - RING + 1)
                elif k == 0:
                    pe.wait_ge(freed, moved)

            def turn_tiles(k, ready, tile):
                for q in range(TT // 4):
                    bank_free(k)
                    for t in range(4):
                        pe.wait_ge(tile_ok, ready(4 * q + t))
                        mm = pe.transpose(aux[:, k % RING, P * t:P * (t + 1)], tile(4 * q + t), ident[:, :])
                    mm.then_inc(fill, 1)
                    k += 1

            pe.wait_ge(consts, 3 + E)
            k = FILLS_MOD
            turn_tiles(k, lambda t: t + 1, lambda t: xn[:, t % 4, :])
            k += FILLS_LN
            pe.wait_ge(w_qkv_in, 16)
            pe.wait_ge(freed, k)
            w_v = w_qkv.rearrange("p (h j d) -> p j h d", j=3, d=DH)[:, 2, :, :]

            def all_v(t, g):
                n = 2 * t + g
                if n >= RING:
                    pe.wait_ge(v_ok, n - RING + 1)
                pe.matmul(score[:, n % RING, :].rearrange("p (h d) -> p h d", d=DH),
                          hT[:, P * t:P * (t + 1)], w_v[:, 8 * g:8 * g + 8, :], start=True, stop=True
                          ).then_inc(v_fill, 1)

            def project(n, c, k, moved):
                bank_free(k, moved)
                pe.matmul(aux[:, k % RING, :], w_head[n][:, :], hT[:, c * BANK:(c + 1) * BANK], start=True, stop=True
                          ).then_inc(fill, 1)

            def query_scores(n, m, k, moved):
                tile, c = divmod(m, NCHUNK)
                bank_free(k, moved)
                if m == 0:
                    pe.wait_ge(freed, k + moved)
                pe.matmul(aux[:, k % RING, :], qhh[n][:, P * tile:P * (tile + 1)], khl[n][:, c * BANK:(c + 1) * BANK],
                          start=True, stop=True).then_inc(fill, 1)

            def turn_maxima(k, moved, heads):
                bank_free(k, moved)
                pe.wait_ge(max_ok, heads)
                pe.transpose(aux[0:KT, k % RING, 0:P], maxq[:, :], ident[:, :]).then_inc(fill, 1)

            pe.wait_ge(w_head_in[0], 16)
            for c in range(NCHUNK):
                project(0, c, k, 0)
                k += 1
            for m in range(MAX_FILLS):
                if m % 2 == 0:
                    all_v(*divmod(m // 2, 2))
                query_scores(0, m, k, 0)
                k += 1
            turn_maxima(k, 0, 1)

            def scores(i, par, t, c):
                f, kt = divmod(t, KT)
                n = 64 * par + 2 * t + c
                keys = slice(P * kt, P * (kt + 1))
                if is_first(i) and n < 2:
                    pe.wait_ge(v_ok, 2 * TT - 1 + n)
                if t == 0 and c == 0:
                    pe.wait_ge(row_in, 16 * (2 * i + par + 1))
                if n >= RING:
                    pe.wait_ge(expd, 128 * i + n - RING + 1)
                elif n < 2 and not is_first(i):
                    pe.wait_ge(expd, 128 * i + n - 1)
                cols = slice(BANK * (2 * f + c), BANK * (2 * f + c + 1))
                o = score[:, n % RING, :]
                pe.matmul(o, khl[par][:, keys], qhh[par][:, cols], start=True, stop=False)
                pe.matmul(o, kh1[par][:, keys], qlm[par][:, cols], start=False, stop=True).then_inc(scored, 1)

            def values(i, par, t):
                f, kt = divmod(t, KT)
                if t == 0:
                    pe.wait_ge(v_in, 16 * (2 * i + par + 1))
                pe.wait_ge(expd, 128 * i + 64 * par + 2 * t + 2)
                if kt == 0 and not (is_first(i) and par == 0):
                    pe.wait_ge(normed, 4 * i + 2 * par + f - 1)
                for c in range(2):
                    mm = pe.matmul(out_acc[DH * c:DH * (c + 1), f, :], v_h[par][:, kt, :],
                                   probs[:, t % PT_RING, BANK * (c ^ par):BANK * ((c ^ par) + 1)],
                                   start=(kt == 0), stop=(kt == KT - 1))
                mm.then_inc(pv_ok, 1)

            def sum_keys(halves, odd, place):
                bank, free, _ = place
                pe.wait_ge(freed, free)
                pe.wait_ge(sums_ok, halves)
                for c in range(2):
                    mm = pe.matmul(bank[DH * c:DH * (c + 1), :], ones[:, 0:DH],
                                   sum_dve[:, BANK * (c ^ odd):BANK * ((c ^ odd) + 1)], start=True, stop=True)
                mm.then_inc(fill, 1)

            def project_out(f, n, place, halves, pairs):
                bank, free, _ = place
                pe.wait_ge(freed, free)
                if n == 0:
                    pe.wait_ge(normed, halves)
                    pe.wait_ge(wo_in, 64 * pairs)
                pe.matmul(bank, wo_pair[:, n, :], attn[:, 2 * f + n, :], start=True, stop=True).then_inc(fill, 1)

            READY = [TT + (2 + HALF_TILES) * f for f in range(2)]

            def back(f, n, place):
                bank, free, _ = place
                pe.wait_ge(freed, free)
                pe.wait_ge(tile_ok, READY[f] + n + 1)
                c = 2 * f + n
                for t in range(4):
                    mm = pe.transpose(bank[:, P * t:P * (t + 1)], y[:, c * BANK + P * t:c * BANK + P * (t + 1)],
                                      ident[:, :])
                mm.then_inc(fill, 1)

            def turned(f, n, place):
                bank, free, _ = place
                pe.wait_ge(freed, free)
                for t in range(4):
                    pe.wait_ge(tile_ok, READY[f] + 2 + 4 * n + t + 1)
                    mm = pe.transpose(bank[:, P * t:P * (t + 1)], xn2[:, 4 * n + t, :], ident[:, :])
                mm.then_inc(fill, 1)

            def gate_logits(f, place):
                bank, _, filled = place
                if f == 0:
                    pe.wait_ge(ffn_in, 64)
                pe.wait_ge(freed, filled - 1)
                for t in range(HALF_TILES):
                    tile = HALF_TILES * f + t
                    mm = pe.matmul(bank[:, E * t:E * (t + 1)], hT[:, P * tile:P * (tile + 1)], wg_sb,
                                   start=True, stop=True)
                mm.then_inc(fill, 1)

            def auxiliary(i, par, t, what, n, k, moved):
                half = 2 * par + t // KT
                if what == "project":
                    if n == 0:
                        pe.wait_ge(w_head_in[1 - par], 16 * (i + par + 1))
                    project(1 - par, n, k, moved)
                elif what == "sums":
                    sum_keys(4 * i + half, ((half - 1) % 4) // 2, ring_fill(k, moved))
                elif what == "output":
                    project_out((half - 1) % 2, n, ring_fill(k, moved), 4 * i + half, i + par)
                elif what == "maximum":
                    query_scores(1 - par, n, k, moved)
                elif what == "turn":
                    turn_maxima(k, moved, 2 * i + par + 2)
                elif what == "back":
                    back(0, n, ring_fill(k, moved))
                elif what == "turned":
                    turned(0, n, ring_fill(k, moved))
                else:
                    gate_logits(0, ring_fill(k, moved))

            def body(i):
                k, moved = 0, turn_fills(i)
                for par in range(2):
                    for t in range(STEPS):
                        work = head_work(i, par, t)
                        scores(i, par, t, 0)
                        for what, n in work[0:1]:
                            auxiliary(i, par, t, what, n, k, moved)
                        scores(i, par, t, 1)
                        for what, n in work[1:2]:
                            auxiliary(i, par, t, what, n, k + 1, moved)
                        if t > 0:
                            values(i, par, t - 1)
                        elif par == 1:
                            values(i, 0, STEPS - 1)
                        elif not is_first(i):
                            values(i - 1, 1, STEPS - 1)
                        for m, (what, n) in enumerate(work[2:]):
                            auxiliary(i, par, t, what, n, k + 2 + m, moved)
                        k += len(work)

            pair_loop(pe, body)
            values(PAIRS - 1, 1, STEPS - 1)
            pe.wait_ge(freed, LAST)
            pe.wait_ge(w_low_ok, 2 * NCHUNK)

            def late(n):
                if n == 3:
                    sum_keys(4 * PAIRS, 1, late_fill(0))
                elif n == 8:
                    for c in range(2):
                        project_out(1, c, late_fill(1 + c), 4 * PAIRS, PAIRS)
                elif n == 11:
                    for c in range(2):
                        back(1, c, late_fill(3 + c))
                elif n in (18, 19):
                    turned(1, n - 18, late_fill(5 + n - 18))
                elif n == 21:
                    gate_logits(1, late_fill(7))

            def experts(j):

                def down(e):
                    pe.wait_ge(up_ok, E * HH * j + HH * (e + 1))
                    if e == 0:
                        pe.wait_ge(weights_ok, 1)
                    if is_first(j) and e == 1:
                        pe.wait_ge(normed, 4 * PAIRS)
                    if not (is_first(j) and e < 2):
                        pe.wait_ge(moe_ok, E * j + e - 1)
                    for t in range(4):
                        for h in range(HH):
                            mm = pe.matmul(out_acc[:, e % 2, P * t:P * (t + 1)], up[:, e % 2, h, P * t:P * (t + 1)],
                                           w3_sb[:, HH * e + h, :], start=(h == 0), stop=(h == HH - 1))
                    mm.then_inc(down_ok, 1)

                for b in range(E * HH):
                    e, h = divmod(b, HH)
                    if not (is_first(j) and b < 2):
                        pe.wait_ge(up_ok, E * HH * j + b - 1)
                    if b == 0:
                        pe.wait_ge(h_low_ok, j + 1 if isinstance(j, int) else NCHUNK)
                    tokens = bass.ds(BANK * j, BANK)
                    units = slice(P * b, P * (b + 1))
                    for n, o in enumerate((score, aux)):
                        pe.matmul(o[:, b % 2, :], w_highs[n][:, units], h_high[:, tokens], start=True, stop=False)
                        pe.matmul(o[:, b % 2, :], w_highs[n][:, units], h_low[:, tokens], start=False, stop=False)
                        mm = pe.matmul(o[:, b % 2, :], w_lows[n][:, units], h_high[:, tokens],
                                       start=False, stop=True)
                    mm.then_inc(hg_ok, 1)
                    if isinstance(j, int):
                        late(E * HH * j + b)
                    if h == HH - 1 and e >= 1:
                        down(e - 1)
                down(E - 1)

            chunk_loop(pe, experts)


INPUTS = ["L0_attn_X", "L0_attn_W_qkv", "L0_attn_W_out", "L0_ffn_Wg", "L0_ffn_W1", "L0_ffn_W2", "L0_ffn_W3",
          "L0_c", "L0_wmod"]


def kernel(**inputs):
    import numpy as np
    import concourse.bacc as bacc
    from concourse.bass_utils import run_bass_kernel_spmd

    nc = bacc.Bacc("TRN2", target_bir_lowering=False, num_devices=1)
    arrays, args = {}, []
    for name in INPUTS:
        a = np.asarray(inputs[name])
        if name == "L0_attn_W_qkv":
            a = a.reshape(a.shape[0], HEADS, DH, 3).transpose(0, 1, 3, 2).reshape(a.shape)
        a = np.ascontiguousarray(a)
        arrays[name + "_dram"] = a
        args.append(nc.dram_tensor(name + "_dram", a.shape, mybir.dt.from_np(a.dtype), kind="ExternalInput").ap())
    out = nc.dram_tensor("out_dram", inputs["L0_attn_X"].shape, F32, kind="ExternalOutput").ap()
    layer(nc, *args, out)
    r = run_bass_kernel_spmd(nc, [arrays], core_ids=[0])
    return r.results[0]["out_dram"]
```
